# Optimizing a Trainium2 kernel written in Bass

```python
import numpy as np
import jax
import jax.numpy as jnp

def _softmax(x, axis=-1):
    return jax.nn.softmax(x, axis=axis)

def _gelu(x):
    return jax.nn.gelu(x, approximate=True)

def _silu(x):
    return jax.nn.silu(x)

def _sigmoid(x):
    return jax.nn.sigmoid(x)

def _layernorm(x, axis=-1, eps=1e-05):
    m = jnp.mean(x, axis=axis, keepdims=True)
    v = jnp.var(x, axis=axis, keepdims=True)
    return (x - m) / jnp.sqrt(v + eps)

def _scatter_add(tgt, idx, src, axis=0):
    return tgt.at[idx].add(src)

def _segment_sum(src, seg, n):
    return jax.ops.segment_sum(src, seg, n)
kernel_name = 'mk_macaron_d2_jaxref_r8_34aa3e'

def setup_inputs(seed: int=0):
    np.random.seed(seed)
    _w = jnp.asarray

    def _L0_attn_setup():
        import jax, jax.numpy as jnp
        import numpy as np
        S = 4
        H = 16

        def _skiparse_1d_single(x, s):
            B, N, C = x.shape
            return x.reshape(B, N // s, s, C).transpose(2, 0, 1, 3).reshape(s * B, N // s, C)

        def _skiparse_1d_single_reverse(x, s, B):
            sB, g, C = x.shape
            return x.reshape(s, B, g, C).transpose(1, 2, 0, 3).reshape(B, g * s, C)
        key = jax.random.key(seed)
        ks = jax.random.split(key, 4)
        B, N, C = (1, 512, 128)
        x = jax.random.normal(ks[0], (B, N, C), dtype=jnp.float32)
        w_qkv = jax.random.normal(ks[1], (C, 3 * C), dtype=jnp.float32) * 0.02
        b_qkv = jnp.zeros((3 * C,), dtype=jnp.float32)
        w_o = jax.random.normal(ks[2], (C, C), dtype=jnp.float32) * 0.02
        b_o = jnp.zeros((C,), dtype=jnp.float32)
        return {'x': x, 'w_qkv': w_qkv, 'b_qkv': b_qkv, 'w_o': w_o, 'b_o': b_o}
    _L0_attn_in = _L0_attn_setup()

    def _L0_ffn_setup():
        import jax, jax.numpy as jnp
        import numpy as np
        NUM_EXPERTS = 8
        HIDDEN = 128
        FFN = 512
        BATCH = 2
        SEQ = 256
        key = jax.random.key(seed)
        k_x, k_g, k_u, k_d = jax.random.split(key, 4)
        scale_in = 1.0 / np.sqrt(HIDDEN)
        scale_mid = 1.0 / np.sqrt(FFN)
        return {'hidden_states': jax.random.normal(k_x, (BATCH, SEQ, HIDDEN), dtype=jnp.float32), 'Wg': jax.random.normal(k_g, (NUM_EXPERTS, HIDDEN, FFN), dtype=jnp.float32) * scale_in, 'Wu': jax.random.normal(k_u, (NUM_EXPERTS, HIDDEN, FFN), dtype=jnp.float32) * scale_in, 'Wd': jax.random.normal(k_d, (NUM_EXPERTS, FFN, HIDDEN), dtype=jnp.float32) * scale_mid}
    _L0_ffn_in = _L0_ffn_setup()

    def _L1_attn_setup():
        import jax, jax.numpy as jnp
        import numpy as np
        DIM = 128
        DIM_HEAD = 64
        HEADS = 8
        INNER = DIM_HEAD * HEADS
        SCALE = DIM_HEAD ** (-0.5)
        COS_SCALE = 1.0

        def layer_norm(x, w, b, eps=1e-05):
            mu = jnp.mean(x, axis=-1, keepdims=True)
            var = jnp.var(x, axis=-1, keepdims=True)
            return (x - mu) * jax.lax.rsqrt(var + eps) * w + b
        key = jax.random.key(seed)
        ks = jax.random.split(key, 6)
        x = jax.random.normal(ks[0], (4, 256, DIM), dtype=jnp.float32)
        Wq = jax.random.normal(ks[1], (DIM, INNER), dtype=jnp.float32) * DIM ** (-0.5)
        Wkv = jax.random.normal(ks[2], (DIM, 2 * DIM_HEAD), dtype=jnp.float32) * DIM ** (-0.5)
        Wo = jax.random.normal(ks[3], (INNER, DIM), dtype=jnp.float32) * INNER ** (-0.5)
        norm_w = jnp.ones((DIM,), jnp.float32)
        norm_b = jnp.zeros((DIM,), jnp.float32)
        out_norm_w = jnp.ones((DIM,), jnp.float32)
        out_norm_b = jnp.zeros((DIM,), jnp.float32)
        return {'x': x, 'Wq': Wq, 'Wkv': Wkv, 'Wo': Wo, 'norm_w': norm_w, 'norm_b': norm_b, 'out_norm_w': out_norm_w, 'out_norm_b': out_norm_b}
    _L1_attn_in = _L1_attn_setup()

    def _L1_ffn_setup():
        import jax, jax.numpy as jnp
        import numpy as np
        B, S, H = (4, 256, 128)
        E, K, INTER = (16, 2, 64)
        ALPHA, LIMIT = (1.702, 7.0)
        key = jax.random.key(seed)
        ks = jax.random.split(key, 6)
        return {'hidden_states': jax.random.normal(ks[0], (B, S, H), jnp.float32), 'router_weight': jax.random.normal(ks[1], (H, E), jnp.float32) * 0.02, 'gate_up_proj': jax.random.normal(ks[2], (E, H, 2 * INTER), jnp.float32) * 0.02, 'gate_up_proj_bias': jax.random.normal(ks[3], (E, 2 * INTER), jnp.float32) * 0.02, 'down_proj': jax.random.normal(ks[4], (E, INTER, H), jnp.float32) * 0.02, 'down_proj_bias': jax.random.normal(ks[5], (E, H), jnp.float32) * 0.02}
    _L1_ffn_in = _L1_ffn_setup()
    _d = {'L0_attn_x': _L0_attn_in['x'], 'L0_attn_w_qkv': _L0_attn_in['w_qkv'], 'L0_attn_b_qkv': _L0_attn_in['b_qkv'], 'L0_attn_w_o': _L0_attn_in['w_o'], 'L0_attn_b_o': _L0_attn_in['b_o'], 'L0_ffn_Wg': _L0_ffn_in['Wg'], 'L0_ffn_Wu': _L0_ffn_in['Wu'], 'L0_ffn_Wd': _L0_ffn_in['Wd'], 'L1_attn_Wq': _L1_attn_in['Wq'], 'L1_attn_Wkv': _L1_attn_in['Wkv'], 'L1_attn_Wo': _L1_attn_in['Wo'], 'L1_attn_norm_w': _L1_attn_in['norm_w'], 'L1_attn_norm_b': _L1_attn_in['norm_b'], 'L1_attn_out_norm_w': _L1_attn_in['out_norm_w'], 'L1_attn_out_norm_b': _L1_attn_in['out_norm_b'], 'L1_ffn_router_weight': _L1_ffn_in['router_weight'], 'L1_ffn_gate_up_proj': _L1_ffn_in['gate_up_proj'], 'L1_ffn_gate_up_proj_bias': _L1_ffn_in['gate_up_proj_bias'], 'L1_ffn_down_proj': _L1_ffn_in['down_proj'], 'L1_ffn_down_proj_bias': _L1_ffn_in['down_proj_bias']}
    _x0 = _d['L0_attn_x']
    _d['L0_attn_x'] = jax.random.normal(jax.random.fold_in(jax.random.key(seed), 1), (2, 2048, 128), dtype=_x0.dtype)
    del _x0
    return _d

def reference(L0_attn_x, L0_attn_w_qkv, L0_attn_b_qkv, L0_attn_w_o, L0_attn_b_o, L0_ffn_Wg, L0_ffn_Wu, L0_ffn_Wd, L1_attn_Wq, L1_attn_Wkv, L1_attn_Wo, L1_attn_norm_w, L1_attn_norm_b, L1_attn_out_norm_w, L1_attn_out_norm_b, L1_ffn_router_weight, L1_ffn_gate_up_proj, L1_ffn_gate_up_proj_bias, L1_ffn_down_proj, L1_ffn_down_proj_bias):

    def _L0_attn_ref(x, w_qkv, b_qkv, w_o, b_o):
        import jax, jax.numpy as jnp
        import numpy as np
        S = 4
        H = 16

        def _skiparse_1d_single(x, s):
            B, N, C = x.shape
            return x.reshape(B, N // s, s, C).transpose(2, 0, 1, 3).reshape(s * B, N // s, C)

        def _skiparse_1d_single_reverse(x, s, B):
            sB, g, C = x.shape
            return x.reshape(s, B, g, C).transpose(1, 2, 0, 3).reshape(B, g * s, C)
        B, N, C = x.shape
        d = C // H
        qkv = x @ w_qkv + b_qkv
        qkv = _skiparse_1d_single(qkv, S)
        q, k, v = jnp.split(qkv, 3, axis=-1)

        def to_heads(t):
            sb, g, _ = t.shape
            return t.reshape(sb, g, H, d).transpose(0, 2, 1, 3)
        q, k, v = (to_heads(q), to_heads(k), to_heads(v))
        scale = 1.0 / jnp.sqrt(jnp.asarray(d, q.dtype))
        scores = jnp.einsum('bhqd,bhkd->bhqk', q, k) * scale
        probs = jax.nn.softmax(scores, axis=-1)
        out = jnp.einsum('bhqk,bhkd->bhqd', probs, v)
        sb, _, g, _ = out.shape
        out = out.transpose(0, 2, 1, 3).reshape(sb, g, C)
        out = _skiparse_1d_single_reverse(out, S, B)
        return out @ w_o + b_o

    def _L0_ffn_ref(hidden_states, Wg, Wu, Wd):
        import jax, jax.numpy as jnp
        import numpy as np
        NUM_EXPERTS = 8
        HIDDEN = 128
        FFN = 512
        BATCH = 2
        SEQ = 256
        B, S, H = hidden_states.shape
        x = hidden_states.reshape(-1, H)

        def expert_step(acc, w):
            wg, wu, wd = w
            h = jax.nn.silu(x @ wg) * (x @ wu)
            return (acc + h @ wd, None)
        acc, _ = jax.lax.scan(expert_step, jnp.zeros_like(x), (Wg, Wu, Wd))
        return acc.reshape(B, S, H)

    def _L1_attn_ref(x, Wq, Wkv, Wo, norm_w, norm_b, out_norm_w, out_norm_b):
        import jax, jax.numpy as jnp
        import numpy as np
        DIM = 128
        DIM_HEAD = 64
        HEADS = 8
        INNER = DIM_HEAD * HEADS
        SCALE = DIM_HEAD ** (-0.5)
        COS_SCALE = 1.0

        def layer_norm(x, w, b, eps=1e-05):
            mu = jnp.mean(x, axis=-1, keepdims=True)
            var = jnp.var(x, axis=-1, keepdims=True)
            return (x - mu) * jax.lax.rsqrt(var + eps) * w + b
        b, n, _ = x.shape
        xn = layer_norm(x, norm_w, norm_b)
        q = xn @ Wq
        kv = xn @ Wkv
        k, v = (kv[..., :DIM_HEAD], kv[..., DIM_HEAD:])
        q = q.reshape(b, n, HEADS, DIM_HEAD).transpose(0, 2, 1, 3) * SCALE
        sim = jnp.einsum('bhid,bjd->bhij', q, k) * COS_SCALE
        attn = jax.nn.softmax(sim.astype(jnp.float32), axis=-1).astype(sim.dtype)
        out = jnp.einsum('bhij,bjd->bhid', attn, v)
        out = out.transpose(0, 2, 1, 3).reshape(b, n, INNER)
        out = out @ Wo
        return layer_norm(out, out_norm_w, out_norm_b)

    def _L1_ffn_ref(hidden_states, router_weight, gate_up_proj, gate_up_proj_bias, down_proj, down_proj_bias):
        import jax, jax.numpy as jnp
        import numpy as np
        B, S, H = (4, 256, 128)
        E, K, INTER = (16, 2, 64)
        ALPHA, LIMIT = (1.702, 7.0)
        b, s, h = hidden_states.shape
        x = hidden_states.reshape(-1, h)
        logits = x @ router_weight
        topk_w, topk_i = jax.lax.top_k(logits, K)
        topk_w = jax.nn.softmax(topk_w, axis=-1)
        one_hot = (topk_i[..., None] == jnp.arange(E)[None, None, :]).astype(topk_w.dtype)
        scores = jnp.einsum('tk,tke->te', topk_w, one_hot)
        gu = jnp.einsum('th,ehf->tef', x, gate_up_proj) + gate_up_proj_bias
        gate = gu[..., ::2]
        up = gu[..., 1::2]
        gate = jnp.minimum(gate, LIMIT)
        up = jnp.clip(up, -LIMIT, LIMIT)
        glu = gate * jax.nn.sigmoid(gate * ALPHA)
        act = (up + 1.0) * glu
        out = jnp.einsum('tei,eih,te->th', act, down_proj, scores)
        out = out + jnp.einsum('te,eh->th', scores, down_proj_bias)
        return out.reshape(b, s, h)
    x = L0_attn_x
    x = x + 0.5 * _L0_ffn_ref(_layernorm(x, axis=-1), L0_ffn_Wg, L0_ffn_Wu, L0_ffn_Wd)
    x = x + _L0_attn_ref(_layernorm(x, axis=-1), L0_attn_w_qkv, L0_attn_b_qkv, L0_attn_w_o, L0_attn_b_o)
    x = x + 0.5 * _L0_ffn_ref(_layernorm(x, axis=-1), L0_ffn_Wg, L0_ffn_Wu, L0_ffn_Wd)
    x = x + 0.5 * _L1_ffn_ref(_layernorm(x, axis=-1), L1_ffn_router_weight, L1_ffn_gate_up_proj, L1_ffn_gate_up_proj_bias, L1_ffn_down_proj, L1_ffn_down_proj_bias)
    x = x + _L1_attn_ref(_layernorm(x, axis=-1), L1_attn_Wq, L1_attn_Wkv, L1_attn_Wo, L1_attn_norm_w, L1_attn_norm_b, L1_attn_out_norm_w, L1_attn_out_norm_b)
    x = x + 0.5 * _L1_ffn_ref(_layernorm(x, axis=-1), L1_ffn_router_weight, L1_ffn_gate_up_proj, L1_ffn_gate_up_proj_bias, L1_ffn_down_proj, L1_ffn_down_proj_bias)
    return x

_drawn_inputs = setup_inputs


def setup_inputs(seed=0):
    import zlib

    import numpy as np

    out = dict(_drawn_inputs(seed))
    spreads = {'L0_attn_b_qkv': (0.0, 0.1),
     'L0_attn_b_o': (0.0, 0.1),
     'L1_attn_norm_w': (1.0, 0.2),
     'L1_attn_norm_b': (0.0, 0.1),
     'L1_attn_out_norm_w': (1.0, 0.2),
     'L1_attn_out_norm_b': (0.0, 0.1)}
    factors = {'L0_attn_w_qkv': 8.0,
     'L1_ffn_router_weight': 6.979,
     'L1_ffn_gate_up_proj': 8.0,
     'L1_ffn_gate_up_proj_bias': 8.0,
     'L1_ffn_down_proj': 8.0,
     'L1_ffn_down_proj_bias': 6.582}
    for name, (base, spread) in spreads.items():
        noise = np.random.default_rng([zlib.crc32(name.encode()), seed]).standard_normal(out[name].shape)
        drawn = base * np.exp(spread * noise) if base else spread * noise
        out[name] = jnp.asarray(drawn.astype(out[name].dtype))
    for name, factor in factors.items():
        out[name] = (out[name] * factor).astype(out[name].dtype)
    return out
```

```python
from contextlib import ExitStack

import concourse.bass as bass
from concourse import mybir

F32, F16, U32 = mybir.dt.float32, mybir.dt.float16, mybir.dt.uint32
ALU, ACT, AX = mybir.AluOpType, mybir.ActivationFunctionType, mybir.AxisListType

P = 128
BATCH, SEQ, C = 2, 2048, 128
STRIDE = 4
GT = SEQ // STRIDE
NG = BATCH * STRIDE
TG = GT // P
NT = NG * TG
EPS = 1e-5

E0, F0 = 8, 512
FCH = F0 // P
FSTEPS = E0 * FCH
E1, I1 = 16, 64
PAIRS = E1 // 2
LIMIT = 7.0

H0, D0 = 16, 8
HPU = 4
H1, D1 = 8, 64
USTEPS = 16
MSC = 64.0
ds = bass.ds


def program(nc, d):
    ctx = ExitStack()
    with ctx:
        def sb(name, shape, dt=F32, at=None):
            return (at or ctx).enter_context(nc.sbuf_tensor(name, shape, dt))

        def sem(name):
            return ctx.enter_context(nc.semaphore(name))

        def sems(tag, names):
            return {n: sem(f"{tag}_{n}") for n in names.split()}

        X = sb("X", [P, NT, C])
        XTH = [sb(f"XTH{i}", [P, NT * P], F16) for i in range(2)]
        XTL = [sb(f"XTL{i}", [P, NT * P], F16) for i in range(2)]
        WG = [sb(f"WG{i}", [P, E0, F0], F16) for i in range(2)]
        WU = [sb(f"WU{i}", [P, E0, F0], F16) for i in range(2)]
        WD = [sb(f"WD{i}", [P, E0, FCH, C], F16) for i in range(2)]
        MG = [sb(f"MG{i}", [P, PAIRS, 2, I1], F16) for i in range(2)]
        MU = [sb(f"MU{i}", [P, PAIRS, 2, I1], F16) for i in range(2)]
        MD = [sb(f"MD{i}", [P, PAIRS, C], F16) for i in range(2)]
        RT = [sb(f"RT{i}", [P, E1], F16) for i in range(2)]
        WQ0 = [sb(f"WQ0{i}", [P, H0 // HPU, 4, 32], F16) for i in range(2)]
        WK0 = [sb(f"WK0{i}", [P, H0 // HPU, 4, 32], F16) for i in range(2)]
        WV0 = [sb(f"WV0{i}", [P, C], F16) for i in range(2)]
        WO0 = [sb(f"WO0{i}", [P, C], F16) for i in range(2)]
        WQ1 = [sb(f"WQ1{i}", [P, H1, 2, D1], F16) for i in range(2)]
        WK1 = [sb(f"WK1{i}", [P, 2, D1], F16) for i in range(2)]
        WV1 = [sb(f"WV1{i}", [P, D1], F16) for i in range(2)]
        WO1 = [sb(f"WO1{i}", [P, H1 // 2, C], F16) for i in range(2)]
        BDR = sb("BDR", [P, C])
        BD = [sb(f"BD{i}", [P, C], F16) for i in range(2)]
        BG = sb("BG", [P, PAIRS])
        BU = sb("BU", [P, PAIRS])
        BU1 = sb("BU1", [P, PAIRS])
        BQ0 = sb("BQ0", [P, H0 // HPU])
        BK0 = sb("BK0", [P, H0 // HPU])
        BV0 = sb("BV0", [P, C])
        BO0 = sb("BO0", [P, C])
        ONW = sb("ONW", [P, C])
        ONB = sb("ONB", [P, C])
        NW = sb("NW", [P, 1])
        NB = sb("NB", [P, 1])
        ID32 = sb("ID32", [P, P])
        ID16 = sb("ID16", [P, P], F16)
        MASK4 = sb("MASK4", [P, 4, HPU])
        MASK = sb("MASK", [P, HPU])
        SEL = sb("SEL", [P, PAIRS, 2, I1], F16)
        IOTA = sb("IOTA", [P, E1])
        SPARE = [sb(f"SPARE{i}", [P, 2]) for i in range(2)]
        NHALF = sb("NHALF", [P, TG])
        BST = sb("BST", [P, TG, 6])
        MV = sb("MV", [P, TG, 2])
        VE = sb("VE", [P, TG])
        RS = sb("RS", [P, TG])
        XN = sb("XN", [P, TG, C])
        XA = sb("XA", [P, GT])
        YT = sb("YT", [P, GT])

        PS = ctx.enter_context(nc.psum_tensor("PS", [P, 8, 512], F32))

        early = ExitStack()
        WST = sb("WST", [P, 4, 3, F0], F32, early)
        RGU = sb("RGU", [P, E1, 2 * I1], F32, early)
        RMD = sb("RMD", [P, PAIRS, C], F32, early)
        RRT = sb("RRT", [P, E1], F32, early)
        RQKV = sb("RQKV", [P, 3, H0 // HPU, 32], F32, early)
        RWO0 = sb("RWO0", [P, C], F32, early)
        RWQ1 = sb("RWQ1", [P, H1, D1], F32, early)
        RKV1 = sb("RKV1", [P, 2, D1], F32, early)
        RWO1 = sb("RWO1", [P, H1 // 2, C], F32, early)
        steps = ExitStack()
        SG = sb("SG", [P, 2, GT], F32, steps)
        H32 = sb("H32", [P, 4, GT], F32, steps)
        HH = sb("HH", [P, 4, GT], F16, steps)
        HL = sb("HL", [P, 4, GT], F16, steps)
        steps.close()
        early.close()

        moe = ExitStack()
        GM = sb("GM", [P, 2, GT], F32, moe)
        UM = sb("UM", [P, 2, GT], F32, moe)
        UC = sb("UC", [P, 2, GT], F32, moe)
        AM = sb("AM", [P, 2, GT], F32, moe)
        S2 = sb("S2", [80, NG * GT], F16, moe)
        LG = sb("LG", [P, TG, E1], F32, moe)
        T8 = sb("T8", [P, TG, 8], F32, moe)
        I8 = sb("I8", [P, TG, 8], U32, moe)
        IF = sb("IF", [P, TG, 2], F32, moe)
        DL = sb("DL", [P, TG], F32, moe)
        TH = sb("TH", [P, TG], F32, moe)
        W12 = sb("W12", [P, 2, TG], F32, moe)
        SA = sb("SA", [P, 2, TG, E1], F32, moe)
        SC = sb("SC", [P, TG, E1], F32, moe)
        S16 = sb("S16", [P, TG, 80], F16, moe)
        moe.close()

        late = ExitStack()
        QA = sb("QA", [P, 4, GT], F16, late)
        QB = sb("QB", [96, 4, GT], F16, late)
        P32 = sb("P32", [P, 4, GT], F32, late)
        PH = sb("PH", [P, 8, GT], F16, late)
        PL = sb("PL", [P, 8, GT], F16, late)
        MX = sb("MX", [P, 2, USTEPS], F32, late)
        MR = sb("MR", [P, TG], F32, late)
        MT = sb("MT", [P, TG, 32], F16, late)
        OS = sb("OS", [P, TG * (2 * D1 + 1)], F32, late)
        RC = sb("RC", [P, 16], F32, late)
        OT = sb("OT", [P, 256], F32, late)
        AO = sb("AO", [P, TG, H1 * D1], F32, late)
        AOH = sb("AOH", [P, GT], F16, late)
        AOL = sb("AOL", [P, GT], F16, late)
        ON = sb("ON", [P, TG, C], F32, late)
        only0, only1 = ExitStack(), ExitStack()
        KM = sb("KM", [P, 4, HPU, GT], F16, only0)
        KR = sb("KR", [P, GT], F16, only0)
        V0 = sb("V0", [P, 4, 4, HPU, 2 * D0 + 1], F16, only0)
        VF = sb("VF", [P, 4, 32], F32, only0)
        only0.close()
        KA = sb("KA", [P, SEQ], F16, only1)
        KB = sb("KB", [96, SEQ], F16, only1)
        V1 = sb("V1", [P, SEQ // P, 2 * D1 + 1], F16, only1)
        only1.close()
        late.close()

        ld_x = [sem(f"ld_x{g}") for g in range(NG)]
        ld_e = [sem(f"ld_e{e}") for e in range(E0)]
        ld_w = sem("ld_w")
        ld_c = sem("ld_c")
        c = sems("const", "zero idn iota whi wlo ehi elo pad pool one bias mask")
        fin = sems("fin", "stats agg var rstd xn xp aff xthi xt")
        out_done = sem("out_done")

        N_LDW = 8
        N_LDC = 17

        def x_dram(t, g):
            return t[g // STRIDE].rearrange("(i p s) c -> s p i c", p=P, s=STRIDE)[g % STRIDE]

        def nf(p, g):
            return 8 * p + g

        def nf_round(p, g, rnd):
            return 8 * p + g if p < 4 else (32 + 2 * g + rnd if p == 4 else 48 + g)

        def carry_pool():
            nc.gpsimd.tensor_tensor(SPARE[1][:, 0:1], NHALF[:, 0:1], NHALF[:, 0:1], ALU.mult)

        def carry_v():
            nc.vector.tensor_copy(SPARE[0][:, 0:1], SPARE[0][:, 1:2])

        def norm_stats(v, p, g, rnd=0):
            r = nf_round(p, g, rnd)
            for i in range(TG):
                src = XN[:, i:i + 1, :] if rnd else X[:, ds(g * TG + i, 1), :]
                nc.vector.bn_stats(BST[:, i, :], src).then_inc(fin["stats"], 1)
            v.wait_ge(fin["stats"], (r + 1) * TG)
            carry_v()
            for i in range(TG):
                nc.vector.bn_aggr(MV[:, i, :], BST[:, i, :]).then_inc(fin["agg"], 1)

        def norm_rstd(pool, p, g, rnd=0):
            r = nf_round(p, g, rnd)
            pool.wait_ge(fin["agg"], (r + 1) * TG)
            carry_pool()
            nc.gpsimd.tensor_scalar(VE[:, :], MV[:, :, 1], EPS, None, ALU.add).then_inc(fin["var"], 1)
            pool.wait_ge(fin["var"], r + 1)
            nc.gpsimd.tensor_tensor(RS[:, :], VE[:, :], NHALF[:, :], ALU.pow).then_inc(fin["rstd"], 1)

        def norm_apply(v, p, g, rnd=0):
            r = nf_round(p, g, rnd)
            v.wait_ge(fin["rstd"], r + 1)
            if not rnd and not (isinstance(g, int) and nf(p, g) == 0):
                v.wait_ge(fin["xp"], nf(p, g))
            for i in range(TG):
                src = XN[:, i:i + 1, :] if rnd else X[:, ds(g * TG + i, 1), :]
                nc.vector.tensor_scalar(XN[:, i:i + 1, :], src, MV[:, i, 0:1], RS[:, i:i + 1],
                                        ALU.subtract, ALU.mult).then_inc(fin["xn"], 1)

        def norm_xn_wait(v, p, g, rnd=0):
            v.wait_ge(fin["xn"], (nf_round(p, g, rnd) + 1) * TG)

        def norm_transpose(pe, p, g, bank):
            norm_xn_wait(pe, p, g, 1 if p == 4 else 0)
            if not (isinstance(g, int) and nf(p, g) == 0):
                pe.wait_ge(fin["xt"], nf(p, g))
            for i in range(TG):
                last = nc.tensor.transpose(PS[:, bank, i * P:(i + 1) * P], XN[:, i, :], ID32[:, :])
            last.then_inc(fin["xp"], 1)

        def norm_hi(a, p, g, bank):
            a.wait_ge(fin["xp"], nf(p, g) + 1)
            dst = XTH[p % 2][:, ds(g * GT, GT)]
            if p == 4:
                nc.scalar.activation(XA[:, :], PS[:, bank, :], ACT.Identity, bias=NB[:, 0:1],
                                     scale=NW[:, 0:1]).then_inc(fin["aff"], 1)
                a.wait_ge(fin["aff"], g + 1)
                nc.scalar.copy(dst, XA[:, :]).then_inc(fin["xthi"], 1)
            else:
                nc.scalar.copy(dst, PS[:, bank, :]).then_inc(fin["xthi"], 1)

        def norm_lo(v, p, g, bank):
            v.wait_ge(fin["xthi"], nf(p, g) + 1)
            src = XA[:, :] if p == 4 else PS[:, bank, :]
            nc.vector.tensor_tensor(XTL[p % 2][:, ds(g * GT, GT)], src, XTH[p % 2][:, ds(g * GT, GT)],
                                    ALU.subtract).then_inc(fin["xt"], 1)

        def split3(out, w, x, **kw):
            start, stop = kw.pop("start", True), kw.pop("stop", True)
            nc.tensor.matmul(out, w[0], x[0], start=start, stop=False, **kw)
            nc.tensor.matmul(out, w[0], x[1], start=False, stop=False, **kw)
            return nc.tensor.matmul(out, w[1], x[0], start=False, stop=stop, **kw)

        def xt(p, g):
            return (XTH[p % 2][:, ds(g * GT, GT)], XTL[p % 2][:, ds(g * GT, GT)])

        def xt_tile(p, g, i):
            return (XTH[p % 2][:, ds(g * GT + i * P, P)], XTL[p % 2][:, ds(g * GT + i * P, P)])

        def drained(eng, p):
            eng.wait_ge(fin["xt"], nf(p, NG))

        def closing(kind):
            if kind == "ffn":
                return dict(evac=3, turn=5, add=7, stats=8, rstd=8, apply=10, tr=12, hi=14, lo=15)
            return dict(evac=4, turn=4, add=4, stats=(4, 5), apply=(5, 6), tr=6, hi=6, lo=7)

        Y_BANK, F_BANK, N_BANK, B_BANK = 4, 5, 6, 7

        def groups(eng, body):
            body(0, True, False)
            with eng.Fori(1, NG) as g:
                body(g, False, False)
            body(NG, False, True)

        def turn_y(pe, s, g):
            pe.wait_ge(s["yt"], g + 1)
            for i in range(TG):
                last = nc.tensor.transpose(PS[:, F_BANK, i * P:(i + 1) * P], YT[:, i * P:(i + 1) * P],
                                           ID32[:, :])
            last.then_inc(s["ft"], 1)

        def evac_y(a, s, g, steps_n):
            a.wait_ge(s["down"], steps_n * (g + 1))
            nc.scalar.mul(YT[:, :], PS[:, Y_BANK, :], 0.5).then_inc(s["yt"], 1)

        def add_x(v, s, g, off):
            v.wait_ge(s["ft"], g + off + 1)
            xg = X[:, ds(g * TG, TG), :].rearrange("p t c -> p (t c)")
            nc.vector.tensor_tensor(xg, xg, PS[:, F_BANK, :], ALU.add).then_inc(s["x"], 1)

        FFN_LAG = 3

        def ffn_pe(pe, s, p, off):
            k_of = closing("ffn")

            def body(g, first, tail):
                for k in range(FSTEPS if not tail else k_of["lo"] + 1):
                    gs = g + off
                    n = gs * FSTEPS + k
                    if not tail:
                        e, f = k // FCH, k % FCH
                        if k == 0:
                            pe.wait_ge(fin["xt"], nf(p, g) + 1)
                        if first and not off and f == 0:
                            pe.wait_ge(c["elo"], e + 1)
                        if not (first and k < 2):
                            pe.wait_ge(s["prod"], n - 1)
                        cs = slice(f * P, (f + 1) * P)
                        x = xt(p, g)
                        split3(PS[:, k % 2, :], (WG[0][:, e, cs], WG[1][:, e, cs]), x)
                        split3(PS[:, 2 + k % 2, :], (WU[0][:, e, cs], WU[1][:, e, cs]), x).then_inc(s["gu"], 1)
                    if (not first or k >= FFN_LAG) and (not tail or k < FFN_LAG):
                        kd = (k - FFN_LAG) % FSTEPS
                        pe.wait_ge(s["h"], n - FFN_LAG + 1)
                        if kd == 0 and not first:
                            pe.wait_ge(s["yt"], gs)
                        e, f = kd // FCH, kd % FCH
                        split3(PS[:, Y_BANK, :], (WD[0][:, e, f, :], WD[1][:, e, f, :]),
                               (HH[:, kd % 4, :], HL[:, kd % 4, :]),
                               start=kd == 0, stop=kd == FSTEPS - 1).then_inc(s["down"], 1)
                    if not first and k == k_of["turn"]:
                        turn_y(pe, s, gs - 1)
                    if not first and k == k_of["tr"]:
                        norm_transpose(pe, p + 1, g - 1, N_BANK)
            groups(pe, body)

        def ffn_act(a, s, p, off):
            k_of = closing("ffn")

            def body(g, first, tail):
                for k in range(FSTEPS if not tail else k_of["lo"] + 1):
                    gs = g + off
                    n = gs * FSTEPS + k
                    if not first and k == k_of["evac"]:
                        evac_y(a, s, gs - 1, FSTEPS)
                    if not tail:
                        a.wait_ge(s["gu"], n + 1)
                        if not (first and k < 2):
                            a.wait_ge(s["prod"], n - 1)
                        nc.scalar.activation(SG[:, k % 2, :], PS[:, k % 2, :], ACT.Silu).then_inc(s["sg"], 1)
                    if (not first or k >= 1) and (not tail or k < 1):
                        a.wait_ge(s["prod"], n)
                        if not (first and k < 5):
                            a.wait_ge(s["down"], n - 4)
                        nc.scalar.copy(HH[:, (k - 1) % 4, :], H32[:, (k - 1) % 4, :]).then_inc(s["hi"], 1)
                    if not first and k == k_of["hi"]:
                        norm_hi(a, p + 1, g - 1, N_BANK)
            groups(a, body)

        def ffn_dve(v, s, p, off):
            k_of = closing("ffn")

            def body(g, first, tail):
                for k in range(FSTEPS if not tail else k_of["lo"] + 1):
                    gs = g + off
                    n = gs * FSTEPS + k
                    if not tail:
                        v.wait_ge(s["sg"], n + 1)
                        if not (first and k < 4):
                            v.wait_ge(s["h"], n - 3)
                        nc.vector.tensor_tensor(H32[:, k % 4, :], SG[:, k % 2, :], PS[:, 2 + k % 2, :],
                                                ALU.mult).then_inc(s["prod"], 1)
                    if (not first or k >= 1) and (not tail or k < 1):
                        v.wait_ge(s["hi"], n)
                        if not (first and k < 5):
                            v.wait_ge(s["down"], n - 4)
                        nc.vector.tensor_tensor(HL[:, (k - 1) % 4, :], H32[:, (k - 1) % 4, :],
                                                HH[:, (k - 1) % 4, :], ALU.subtract).then_inc(s["h"], 1)
                    if not first and k == k_of["add"]:
                        add_x(v, s, g - 1, off)
                    if not first and k == k_of["stats"]:
                        v.wait_ge(s["x"], gs)
                        carry_v()
                        norm_stats(v, p + 1, g - 1)
                    if not first and k == k_of["apply"]:
                        norm_apply(v, p + 1, g - 1)
                    if not first and k == k_of["lo"]:
                        norm_lo(v, p + 1, g - 1, N_BANK)
            groups(v, body)

        def norms_pool(pool, p):
            with pool.Fori(0, NG) as g:
                norm_rstd(pool, p, g)

        MOE_LAG = 4

        def route_logits(pe, s, p, gx, off):
            g = gx + off
            pe.wait_ge(fin["xt"], nf(p, gx) + 1)
            if not (isinstance(g, int) and g == 0):
                pe.wait_ge(s["s2"], g)
            for i in range(TG):
                x = xt_tile(p, gx, i)
                last = split3(PS[:, F_BANK, i * E1:(i + 1) * E1], x, (RT[0][:, :], RT[1][:, :]))
            last.then_inc(s["lg"], 1)

        def route_top(v, s, g):
            v.wait_ge(s["lg"], g + 1)
            nc.vector.tensor_copy(LG[:, :, :], PS[:, F_BANK, 0:TG * E1].rearrange("p (t e) -> p t e", e=E1))\
                .then_inc(s["lgs"], 1)
            v.wait_ge(s["lgs"], g + 1)
            carry_v()
            for i in range(TG):
                nc.vector.max(T8[:, i, :], LG[:, i, :]).then_inc(s["t8"], 1)

        def route_index(v, s, g):
            v.wait_ge(s["t8"], TG * (g + 1))
            if not (isinstance(g, int) and g == 0):
                v.wait_ge(s["th"], g)
                v.wait_ge(s["sa"], g)
            nc.vector.tensor_tensor(DL[:, :], T8[:, :, 0], T8[:, :, 1], ALU.subtract).then_inc(s["dl"], 1)
            for i in range(TG):
                nc.vector.max_index(I8[:, i, :], T8[:, i, :], LG[:, i, :]).then_inc(s["i8"], 1)
            v.wait_ge(s["i8"], TG * (g + 1))
            nc.vector.tensor_copy(IF[:, :, :], I8[:, :, 0:2]).then_inc(s["ifl"], 1)

        def route_tanh(a, s, g):
            a.wait_ge(s["dl"], g + 1)
            if not (isinstance(g, int) and g == 0):
                a.wait_ge(s["w12"], 2 * g)
            nc.scalar.activation(TH[:, :], DL[:, :], ACT.Tanh, scale=0.5).then_inc(s["th"], 1)

        def route_scores(pool, s, g):
            pool.wait_ge(s["th"], g + 1)
            carry_pool()
            nc.gpsimd.tensor_scalar(W12[:, 0, :], TH[:, :], 0.5, 0.5, ALU.mult, ALU.add).then_inc(s["w12"], 1)
            nc.gpsimd.tensor_scalar(W12[:, 1, :], TH[:, :], -0.5, 0.5, ALU.mult, ALU.add).then_inc(s["w12"], 1)
            pool.wait_ge(s["w12"], 2 * g + 2)
            pool.wait_ge(s["ifl"], g + 1)
            carry_pool()
            for r in range(2):
                for i in range(TG):
                    last = nc.gpsimd.tensor_scalar(SA[:, r, i, :], IOTA[:, :], IF[:, i, r:r + 1],
                                                   W12[:, r, i:i + 1], ALU.is_equal, ALU.mult)
            last.then_inc(s["sa"], 1)
            pool.wait_ge(s["sa"], g + 1)
            nc.gpsimd.tensor_tensor(SC[:, :, :], SA[:, 0, :, :], SA[:, 1, :, :], ALU.add).then_inc(s["sc"], 1)
            pool.wait_ge(s["sc"], g + 1)
            if not (isinstance(g, int) and g == 0):
                pool.wait_ge(s["st"], g)
            carry_pool()
            nc.gpsimd.tensor_copy(S16[:, :, 0:E1], SC[:, :, :]).then_inc(s["s16h"], 1)
            pool.wait_ge(s["s16h"], g + 1)
            nc.gpsimd.tensor_tensor(S16[:, :, 64:64 + E1], SC[:, :, :], S16[:, :, 0:E1],
                                    ALU.subtract).then_inc(s["s16"], 1)

        def route_turn(pe, s, g):
            pe.wait_ge(s["s16"], g + 1)
            pe.wait_ge(s["lgs"], g + 1)
            bank = PS[0:80, F_BANK, :].bitcast(F16)
            for i in range(TG):
                last = nc.tensor.transpose(bank[:, i * P:(i + 1) * P], S16[:, i, :], ID16[:, :])
            last.then_inc(s["st"], 1)

        def route_keep(a, s, g, off):
            a.wait_ge(s["st"], g + off + 1)
            nc.scalar.copy(S2[:, ds(g * GT, GT)], PS[0:80, F_BANK, :].bitcast(F16)[:, 0:GT]).then_inc(s["s2"], 1)

        def moe_groups(eng, body):
            body(0, True, False)
            with eng.Fori(1, NG - 1) as g:
                body(g, False, False)
            body(NG - 1, False, False)
            body(NG, False, True)

        def ahead(g):
            return not (isinstance(g, int) and g + 1 >= NG)

        def moe_pe(pe, s, p, off):
            k_of = closing("moe")
            route_logits(pe, s, p, 0, off)
            route_turn(pe, s, off)

            def body(g, first, tail):
                for k in range(PAIRS if not tail else PAIRS):
                    gs = g + off
                    n = gs * PAIRS + k
                    if not tail:
                        if k == 0:
                            pe.wait_ge(fin["xt"], nf(p, g) + 1)
                        if not (first and k < 2):
                            pe.wait_ge(s["g"], n - 1)
                            pe.wait_ge(s["u"], n - 1)
                        x = xt(p, g)
                        w = [m[:, k, :, :].rearrange("p e i -> p (e i)") for m in MG + MU]
                        split3(PS[:, k % 2, :], w[0:2], x)
                        split3(PS[:, 2 + k % 2, :], w[2:4], x).then_inc(s["gu"], 1)
                    if (not first or k >= 1) and (not tail or k < 1):
                        kb, gb = (k - 1) % PAIRS, g if k >= 1 else g - 1
                        if kb == 0:
                            pe.wait_ge(s["s2"], gb + off + 1)
                        if not (first and k < 2):
                            pe.wait_ge(s["prod"], n - 1)
                        nc.tensor.matmul(PS[:, B_BANK, :], SEL[0:80, kb, :, :].rearrange("p e i -> p (e i)"),
                                         S2[:, ds(gb * GT, GT)], start=True, stop=True).then_inc(s["b"], 1)
                    if (not first or k >= MOE_LAG) and (not tail or k < MOE_LAG):
                        kd, gd = (k - MOE_LAG) % PAIRS, g if k >= MOE_LAG else g - 1
                        if kd == 0:
                            if not first:
                                pe.wait_ge(s["yt"], gs)
                            s2 = S2[:, ds(gd * GT, GT)]
                            for part in BD:
                                nc.tensor.matmul(PS[:, Y_BANK, :], part[0:80, :], s2, start=part is BD[0],
                                                 stop=False)
                        pe.wait_ge(s["h"], n - MOE_LAG + 1)
                        split3(PS[:, Y_BANK, :], (MD[0][:, kd, :], MD[1][:, kd, :]),
                               (HH[:, kd % 4, :], HL[:, kd % 4, :]),
                               start=False, stop=kd == PAIRS - 1).then_inc(s["down"], 1)
                    if not tail and k == 1 and ahead(g):
                        route_logits(pe, s, p, g + 1, off)
                    if not first and k == k_of["turn"]:
                        if not tail and ahead(g):
                            pe.wait_ge(s["lgs"], gs + 2)
                        turn_y(pe, s, gs - 1)
                    if not first and k == k_of["tr"]:
                        if p < 5:
                            norm_transpose(pe, p + 1, g - 1, N_BANK)
                    if not first and not tail and k == 0:
                        route_turn(pe, s, gs)
            moe_groups(pe, body)

        def moe_act(a, s, p, off):
            k_of = closing("moe")
            route_tanh(a, s, off)
            route_keep(a, s, 0, off)

            def body(g, first, tail):
                for k in range(PAIRS):
                    gs = g + off
                    n = gs * PAIRS + k
                    if not first and k == k_of["evac"]:
                        evac_y(a, s, gs - 1, PAIRS)
                    if not tail:
                        a.wait_ge(s["gu"], n + 1)
                        if not (first and k < 2):
                            a.wait_ge(s["uc"], n - 1)
                        nc.scalar.activation(UM[:, k % 2, :], PS[:, 2 + k % 2, :], ACT.Identity,
                                             bias=BU1[:, k:k + 1]).then_inc(s["u"], 1)
                    if (not first or k >= 2) and (not tail or k < 2):
                        a.wait_ge(s["prod"], n - 1)
                        if not (first and k < 6):
                            a.wait_ge(s["down"], n - 5)
                        nc.scalar.copy(HH[:, (k - 2) % 4, :], H32[:, k % 2, :]).then_inc(s["hi"], 1)
                    if not tail:
                        a.wait_ge(s["g"], n + 1)
                        if not (first and k < 2):
                            a.wait_ge(s["a"], n - 1)
                        nc.scalar.activation(SG[:, k % 2, :], GM[:, k % 2, :], ACT.Gelu_apprx_sigmoid)\
                            .then_inc(s["sg"], 1)
                    if not tail and k == 3 and ahead(g):
                        route_tanh(a, s, gs + 1)
                    if not first and k == k_of["hi"] and p < 5:
                        norm_hi(a, p + 1, g - 1, N_BANK)
                    if not first and not tail and k == 0:
                        route_keep(a, s, g, off)
            moe_groups(a, body)

        def moe_pool(pool, s, p, off):
            k_of = closing("moe")
            route_scores(pool, s, off)

            def body(g, first, tail):
                for k in range(PAIRS):
                    gs = g + off
                    n = gs * PAIRS + k
                    if (not first or k >= 2) and (not tail or k < 2):
                        pool.wait_ge(s["hi"], n - 1)
                        if not (first and k < 6):
                            pool.wait_ge(s["down"], n - 5)
                        nc.gpsimd.tensor_tensor(HL[:, (k - 2) % 4, :], H32[:, k % 2, :],
                                                HH[:, (k - 2) % 4, :], ALU.subtract).then_inc(s["h"], 1)
                    for rnd in range(2):
                        if not first and k == k_of["stats"][rnd] and p < 5:
                            norm_rstd(pool, p + 1, g - 1, rnd)
                    if not tail and k == 5 and ahead(g):
                        route_scores(pool, s, gs + 1)
            moe_groups(pool, body)

        def moe_dve(v, s, p, off):
            k_of = closing("moe")
            route_top(v, s, off)
            route_index(v, s, off)

            def body(g, first, tail):
                for k in range(PAIRS):
                    gs = g + off
                    n = gs * PAIRS + k
                    one_back = (not first or k >= 1) and (not tail or k < 1)
                    two_back = (not first or k >= 2) and (not tail or k < 2)
                    if one_back:
                        v.wait_ge(s["u"], n)
                        if not (first and k < 3):
                            v.wait_ge(s["a"], n - 2)
                        nc.vector.tensor_scalar(UC[:, (k - 1) % 2, :], UM[:, (k - 1) % 2, :], LIMIT + 1.0,
                                                1.0 - LIMIT, ALU.min, ALU.max).then_inc(s["uc"], 1)
                    if two_back:
                        v.wait_ge(s["b"], n - 1)
                        v.wait_ge(s["a"], n - 1)
                        if not (first and k < 4):
                            v.wait_ge(s["h"], n - 3)
                        nc.vector.tensor_tensor(H32[:, k % 2, :], AM[:, k % 2, :], PS[:, B_BANK, :],
                                                ALU.mult).then_inc(s["prod"], 1)
                    if not tail:
                        v.wait_ge(s["gu"], n + 1)
                        if not (first and k < 2):
                            v.wait_ge(s["sg"], n - 1)
                        nc.vector.tensor_scalar(GM[:, k % 2, :], PS[:, k % 2, :], BG[:, k:k + 1], LIMIT,
                                                ALU.add, ALU.min).then_inc(s["g"], 1)
                    if one_back:
                        v.wait_ge(s["sg"], n)
                        v.wait_ge(s["uc"], n)
                        nc.vector.tensor_tensor(AM[:, (k - 1) % 2, :], SG[:, (k - 1) % 2, :],
                                                UC[:, (k - 1) % 2, :],
                                                ALU.mult).then_inc(s["a"], 1)
                    if not tail and k == 2 and ahead(g):
                        route_top(v, s, gs + 1)
                    if not tail and k == 3 and ahead(g):
                        route_index(v, s, gs + 1)
                    if not first and k == k_of["add"]:
                        add_x(v, s, g - 1, off)
                    if not first and k == k_of["stats"][0] and p < 5:
                        v.wait_ge(s["x"], gs)
                        carry_v()
                        norm_stats(v, p + 1, g - 1)
                    if not first and k == k_of["apply"][0] and p < 5:
                        norm_apply(v, p + 1, g - 1)
                        norm_xn_wait(v, p + 1, g - 1)
                        carry_v()
                        norm_stats(v, p + 1, g - 1, 1)
                    if not first and k == k_of["apply"][1] and p < 5:
                        norm_apply(v, p + 1, g - 1, 1)
                    if not first and k == k_of["lo"] and p < 5:
                        norm_lo(v, p + 1, g - 1, N_BANK)
            moe_groups(v, body)

        S_BANK, M_BANK, O_BANK, A_BANK, W_BANK = 0, 2, 4, 6, 7
        MLEAD = 22
        AVLAG = 5
        SPLIT_LAG = 2
        RP = 8

        def att(kind):
            if kind == 0:
                return dict(
                    kind=0, p=1, upg=H0 // HPU, scale=float(D0) ** -0.5, groups=NG, outer=1,
                    k_pe=0, k_ev=1, q_pe=2, q_ev=3, v_pe=4, v_ev=5, m_nm=11, m_pe=12, m_ev=13,
                    o_ev=5, o_post=7, t_pe=9, t_ev=10, w_pe=11, rounds=1, tail=3,
                    x_w=1, x_s=1, st_w=1, st_s=3, ap_w=1, ap_s=7, tr_w=1, tr_s=9, hi_s=10, lo_s=11)
            return dict(
                kind=1, p=4, upg=H1, scale=float(D1) ** -0.5, groups=NG // BATCH, outer=BATCH,
                q_pe=1, q_ev=2, m_nm=11, m_pe=12, m_ev=13, o_ev=5, o_post=7,
                t_pe=9, t_ev=10, w_pe=11, rounds=H1 // 2, tail=5,
                x_w=4, x_s=0, st_w=4, st_s=6, ap_w=4, ap_s=9, tr_w=4, tr_s=11, hi_s=12, lo_s=13)

        def att_run(eng, q, body, before=None):
            def run(base):
                eng.wait_ge(fin["xt"], nf(q["p"] + 1, base))
                if before:
                    before(base)
                body(base, True, False)
                with eng.Fori(1, q["groups"] - 1) as g:
                    body(base + g, False, False)
                body(base + (q["groups"] - 1), False, True)
            if q["outer"] == 1:
                run(0)
            else:
                with eng.Fori(0, q["outer"]) as b:
                    run(b * q["groups"])

        def units(q, first, last):
            return range(-2 if first else 0, q["upg"] + (q["tail"] if last else 0))

        def live(q, uu, first, last):
            return not (first and uu < 0) and not (last and uu >= q["upg"])

        def on_act(c_):
            return c_ % 4 != 3

        def three_of(base, c_):
            return base * 3 + (3 * (c_ // 4) + min(c_ % 4 + 1, 3))

        def wait_steps(eng, q, sem3, sem1, u4, c_):
            if on_act(c_):
                eng.wait_ge(sem3, three_of(u4, c_))
            else:
                eng.wait_ge(sem1, u4 + (c_ // 4 + 1))

        def positive(q, g, uu, c_, first):
            return not (first and uu * USTEPS + c_ < 0)

        def closing_pos(q, g, uu, first, last):
            if uu < 0:
                return None
            if uu >= q["upg"]:
                return g, uu - q["upg"]
            return None if first else (g - 1, uu)

        def att_pe(pe, s, q):
            def prep_qkv0(g, uu, u, what, first):
                hg = uu % q["upg"]
                gg = g + (uu // q["upg"])
                x = xt(q["p"], gg)
                if what == "k":
                    pe.wait_ge(fin["xt"], nf(q["p"], gg) + 1)
                    if not (first and uu < 1):
                        pe.wait_ge(s["vlo"], u)
                    if not (first and uu < 2):
                        pe.wait_ge(s["mrow"], u - 1)
                    split3(PS[:, A_BANK, :], [w[:, hg, :, :].rearrange("p r d -> p (r d)") for w in WK0],
                           x).then_inc(s["kp"], 1)
                elif what == "q":
                    pe.wait_ge(s["klo"], u + 1)
                    split3(PS[:, A_BANK, :], [w[:, hg, :, :].rearrange("p r d -> p (r d)") for w in WQ0],
                           x).then_inc(s["qp"], 1)
                else:
                    pe.wait_ge(s["qlo"], u + 1)
                    for i in range(TG):
                        last = split3(PS[:, A_BANK, i * 32:(i + 1) * 32], xt_tile(q["p"], gg, i),
                                      [w[:, hg * 32:(hg + 1) * 32] for w in WV0])
                    last.then_inc(s["vp"], 1)

            def prep_q1(g, uu, u, first):
                h = uu % q["upg"]
                gg = g + (uu // q["upg"])
                if not (first and uu < 1):
                    pe.wait_ge(s["qlo"], u)
                if not (first and uu < 2):
                    pe.wait_ge(s["mrow"], u - 1)
                split3(PS[:, A_BANK, :], [w[:, h, :, :].rearrange("p r d -> p (r d)") for w in WQ1],
                       xt(q["p"], gg)).then_inc(s["qp"], 1)

            def maxima(g, uu, u, pos, first):
                m16 = u * USTEPS + pos
                if pos == 0:
                    pe.wait_ge(s["qlo"], u + 1)
                    if q["kind"] == 0:
                        pe.wait_ge(s["km"], u * HPU + HPU)
                if not (first and uu * USTEPS + pos < 2):
                    pe.wait_ge(s["mx"], m16 - 1)
                r = uu % 4
                bank = PS[:, M_BANK + pos % 2, :]
                if q["kind"] == 0:
                    j, i = pos // 4, pos % 4
                    mm = nc.tensor.matmul(bank, QA[:, r, i * P:(i + 1) * P], KM[:, r, j, :], start=True, stop=True)
                else:
                    i, kc = pos // 4, pos % 4
                    mm = nc.tensor.matmul(bank, QA[:, r, i * P:(i + 1) * P], KA[:, kc * GT:(kc + 1) * GT],
                                          start=True, stop=True)
                mm.then_inc(s["sm"], 1)

            def max_rows(u, made):
                pe.wait_ge(s["nm"], u + 1)
                if made:
                    pe.wait_ge(s["vlo"] if q["kind"] == 0 else s["qlo"], u + 2)
                lo = 96 if q["kind"] == 0 else 64
                for i in range(TG):
                    last = nc.tensor.matmul(PS[lo:lo + 32, A_BANK, i * P:(i + 1) * P], MT[:, i, :], ID16[:, :],
                                            start=True, stop=True)
                last.then_inc(s["mt"], 1)

            def scores(g, uu, u, st, first):
                if st == 0:
                    pe.wait_ge(s["mrow"], u + 1)
                if positive(q, g, uu, st - 2, first):
                    if on_act(st - 2):
                        pe.wait_ge(s["pha"], three_of(u * 4, st - 2))
                    else:
                        pe.wait_ge(s["p32"], u * USTEPS + st - 1)
                r = uu % 4
                bank = PS[:, S_BANK + st % 2, :]
                if q["kind"] == 0:
                    j, kt = st // 4, st % 4
                    nc.tensor.matmul(bank, KM[:, r, j, kt * P:(kt + 1) * P], QA[:, r, :],
                                     start=True, stop=True).then_inc(s["st"], 1)
                else:
                    nc.tensor.matmul(bank, KA[:, st * P:(st + 1) * P], QA[:, r, :], start=True, stop=False)
                    nc.tensor.matmul(bank, KB[:, st * P:(st + 1) * P], QB[:, r, :], start=False,
                                     stop=True).then_inc(s["st"], 1)

            def values(g, uu, u, st, first):
                if on_act(st):
                    pe.wait_ge(s["plp"], three_of(u * 4, st))
                else:
                    pe.wait_ge(s["plv"], u * 4 + st // 4 + 1)
                r = st % RP
                if q["kind"] == 0:
                    j, kt = st // 4, st % 4
                    if st == 0 and not (first and uu < 2):
                        pe.wait_ge(s["oev"], u - 1)
                    w = 2 * D0 + 1
                    v = V0[:, uu % 4, kt, j, :]
                    for i in range(TG):
                        o = (i * HPU + j) * w
                        bank = PS[:, O_BANK + uu % 2, :]
                        nc.tensor.matmul(bank[:, o:o + w], PH[:, r, i * P:(i + 1) * P], v,
                                         start=st == 0 and i == 0, stop=False, skip_group_check=True)
                        last = nc.tensor.matmul(bank[:, o + D0:o + w], PL[:, r, i * P:(i + 1) * P], v[:, D0:w],
                                                start=False, stop=kt == 3, skip_group_check=True)
                else:
                    if st == 0 and not (first and uu < 1):
                        pe.wait_ge(s["oev"], u)
                    w = 2 * D1 + 1
                    v = V1[:, st, :]
                    for i in range(TG):
                        bank = PS[:, O_BANK + i // 2, :]
                        o = (i % 2) * w
                        nc.tensor.matmul(bank[:, o:o + w], PH[:, r, i * P:(i + 1) * P], v,
                                         start=st == 0 and i % 2 == 0, stop=False, skip_group_check=True)
                        last = nc.tensor.matmul(bank[:, o + D1:o + w], PL[:, r, i * P:(i + 1) * P], v[:, D1:w],
                                                start=False, stop=st == USTEPS - 1, skip_group_check=True)
                last.then_inc(s["av"], 1)

            def turn_out(gg, rnd, u_next):
                pe.wait_ge(s["post"], (gg + 1) * q["upg"])
                if q["kind"] == 0:
                    pe.wait_ge(s["vlo"], u_next)
                else:
                    pe.wait_ge(s["qlo"], u_next)
                for i in range(TG):
                    last = nc.tensor.transpose(PS[:, A_BANK, i * P:(i + 1) * P], AO[:, i, rnd * P:(rnd + 1) * P],
                                               ID32[:, :])
                last.then_inc(s["aot"], 1)

            def project_out(gg, rnd):
                pe.wait_ge(s["aolo"], gg * q["rounds"] + rnd + 1)
                if rnd == 0:
                    pe.wait_ge(fin["xt"], nf(q["p"] + 1, gg))
                w = WO0 if q["kind"] == 0 else WO1
                for i in range(TG):
                    a = [t[:, i * P:(i + 1) * P] for t in (AOH, AOL)]
                    m = [t[:, :] if q["kind"] == 0 else t[:, rnd, :] for t in w]
                    last = split3(PS[:, W_BANK, i * C:(i + 1) * C], a, m, start=rnd == 0 and i == 0,
                                  stop=rnd == q["rounds"] - 1, skip_group_check=True)
                last.then_inc(s["wo"], 1)

            def prelude1(base):
                for i4 in range(q["groups"]):
                    gg = base + i4
                    pe.wait_ge(fin["xt"], nf(q["p"], gg) + 1)
                    if i4:
                        pe.wait_ge(s["kfree"], gg)
                    split3(PS[:, A_BANK, :], [w[:, :, :].rearrange("p r d -> p (r d)") for w in WK1],
                           xt(q["p"], gg)).then_inc(s["kp"], 1)
                    if i4:
                        pe.wait_ge(s["vfree"], gg)
                    for i in range(TG):
                        last = split3(PS[:, W_BANK, i * D1:(i + 1) * D1], xt_tile(q["p"], gg, i),
                                      [w[:, :] for w in WV1])
                    last.then_inc(s["vp"], 1)
                pe.wait_ge(s["kfree"], base + q["groups"])
                pe.wait_ge(s["vfree"], base + q["groups"])

            def body(g, first, last):
                for uu in units(q, first, last):
                    u = g * q["upg"] + uu
                    for st in range(USTEPS):
                        n = uu * USTEPS + st
                        if live(q, uu + 2, first, last) and q["kind"] == 0:
                            for what, at in (("k", q["k_pe"]), ("q", q["q_pe"]), ("v", q["v_pe"])):
                                if st == at:
                                    prep_qkv0(g, uu + 2, u + 2, what, first)
                        if live(q, uu + 2, first, last) and q["kind"] == 1 and st == q["q_pe"]:
                            prep_q1(g, uu + 2, u + 2, first)
                        mu, mpos = (n + MLEAD) // USTEPS, (n + MLEAD) % USTEPS
                        if live(q, mu, first, last):
                            maxima(g, mu, g * q["upg"] + mu, mpos, first)
                        if live(q, uu + 1, first, last) and st == q["m_pe"]:
                            max_rows(u + 1, live(q, uu + 2, first, last))
                        if live(q, uu, first, last):
                            scores(g, uu, u, st, first)
                        vu, vst = (n - AVLAG) // USTEPS, (n - AVLAG) % USTEPS
                        if live(q, vu, first, last):
                            values(g, vu, g * q["upg"] + vu, vst, first)
                        pos = closing_pos(q, g, uu, first, last)
                        if pos:
                            gg, w = pos
                            u_made = (g * q["upg"] + min(uu + 3, q["upg"])) if last else u + 3
                            if st == q["t_pe"] and w < q["rounds"]:
                                turn_out(gg, w, u_made)
                            if st == q["w_pe"] and w < q["rounds"]:
                                project_out(gg, w)
                            if w == q["tr_w"] and st == q["tr_s"]:
                                norm_transpose(pe, q["p"] + 1, gg, W_BANK)
            att_run(pe, q, body, prelude1 if q["kind"] == 1 else None)

        def att_act(a, s, q):
            def body(g, first, last):
                for uu in units(q, first, last):
                    u = g * q["upg"] + uu
                    for st in range(USTEPS):
                        n = uu * USTEPS + st
                        ov = uu - 1
                        if live(q, ov, first, last) and st == q["o_ev"]:
                            uo = g * q["upg"] + ov
                            a.wait_ge(s["av"], uo * USTEPS + USTEPS)
                            if not (first and ov < 1):
                                a.wait_ge(s["post"], uo)
                            if q["kind"] == 0:
                                wd = TG * HPU * (2 * D0 + 1)
                                nc.scalar.copy(OS[:, 0:wd], PS[:, O_BANK + ov % 2, 0:wd]).then_inc(s["oev"], 1)
                            else:
                                wd = 2 * (2 * D1 + 1)
                                nc.scalar.copy(OS[:, 0:2 * wd].rearrange("p (b n) -> p b n", b=2),
                                               PS[:, O_BANK:O_BANK + 2, 0:wd]).then_inc(s["oev"], 1)
                        u2 = u + 2
                        if live(q, uu + 2, first, last):
                            r = (uu + 2) % 4
                            hg = (uu + 2) % q["upg"]
                            if q["kind"] == 0 and st == q["k_ev"]:
                                a.wait_ge(s["kp"], u2 + 1)
                                if not (first and uu + 2 < 1):
                                    a.wait_ge(s["km"], u2 * HPU)
                                nc.scalar.activation(KR[:, :], PS[:, A_BANK, :], ACT.Identity,
                                                     bias=BK0[:, hg:hg + 1]).then_inc(s["khi"], 1)
                            if q["kind"] == 0 and st == q["q_ev"]:
                                a.wait_ge(s["qp"], u2 + 1)
                                nc.scalar.activation(QA[:, r, :], PS[:, A_BANK, :], ACT.Identity,
                                                     bias=BQ0[:, hg:hg + 1]).then_inc(s["qhi"], 1)
                            if q["kind"] == 1 and st == q["q_ev"]:
                                a.wait_ge(s["qp"], u2 + 1)
                                nc.scalar.copy(QA[:, r, :], PS[:, A_BANK, :]).then_inc(s["qhi"], 1)
                        if live(q, uu, first, last):
                            m = u * USTEPS + st
                            a.wait_ge(s["st"], m + 1)
                            if positive(q, g, uu, st - 4, first):
                                wait_steps(a, q, s["plp"], s["plv"], u * 4, st - 4)
                            nc.scalar.activation(P32[:, st % 4, :], PS[:, S_BANK + st % 2, :], ACT.Exp,
                                                 scale=q["scale"]).then_inc(s["p32"], 1)
                            if on_act(st):
                                if positive(q, g, uu, st - RP, first):
                                    a.wait_ge(s["av"], m - (RP - 1))
                                nc.scalar.activation(PH[:, st % RP, :], PS[:, S_BANK + st % 2, :], ACT.Exp,
                                                     scale=q["scale"]).then_inc(s["pha"], 1)
                        pos = closing_pos(q, g, uu, first, last)
                        if pos:
                            gg, w = pos
                            if st == q["t_ev"] and w < q["rounds"]:
                                a.wait_ge(s["aot"], gg * q["rounds"] + w + 1)
                                if w:
                                    a.wait_ge(s["wo"], gg * q["rounds"] + w)
                                nc.scalar.copy(AOH[:, :], PS[:, A_BANK, :]).then_inc(s["aohi"], 1)
                            if w == q["tr_w"] and st == q["hi_s"]:
                                norm_hi(a, q["p"] + 1, gg, W_BANK)

            def prelude1(base):
                for i4 in range(q["groups"]):
                    gg = base + i4
                    a.wait_ge(s["kp"], gg + 1)
                    nc.scalar.copy(KA[:, ds(i4 * GT, GT)], PS[:, A_BANK, :]).then_inc(s["khi"], 1)
                    a.wait_ge(s["vp"], gg + 1)
                    nc.scalar.copy(V1[:, ds(i4 * TG, TG), D1:2 * D1],
                                   PS[:, W_BANK, 0:TG * D1].rearrange("p (t d) -> p t d", d=D1))\
                        .then_inc(s["vhi"], 1)
            att_run(a, q, body, prelude1 if q["kind"] == 1 else None)

        def att_pool(pool, s, q):
            def body(g, first, last):
                for uu in units(q, first, last):
                    u = g * q["upg"] + uu
                    for st in range(USTEPS):
                        if live(q, uu, first, last) and on_act(st):
                            pool.wait_ge(s["pha"], three_of(u * 4, st))
                            if positive(q, g, uu, st - RP, first):
                                pool.wait_ge(s["av"], u * USTEPS + (st - RP + 1))
                            nc.gpsimd.tensor_tensor(PL[:, st % RP, :], P32[:, st % 4, :], PH[:, st % RP, :],
                                                    ALU.subtract).then_inc(s["plp"], 1)
                        pos = closing_pos(q, g, uu, first, last)
                        if pos:
                            gg, w = pos
                            if q["kind"] == 1 and w == q["x_w"] and st == q["x_s"]:
                                pool.wait_ge(s["oagg"], (gg + 1) * TG)
                                carry_pool()
                                nc.gpsimd.tensor_scalar(VE[:, :], MV[:, :, 1], EPS, None, ALU.add)\
                                    .then_inc(s["ovar"], 1)
                                pool.wait_ge(s["ovar"], gg + 1)
                                nc.gpsimd.tensor_tensor(RS[:, :], VE[:, :], NHALF[:, :], ALU.pow)\
                                    .then_inc(s["orstd"], 1)
                            if w == q["st_w"] and st == q["st_s"]:
                                norm_rstd(pool, q["p"] + 1, gg)
            att_run(pool, q, body)

        def att_dve(v, s, q):
            def body(g, first, last):
                for uu in units(q, first, last):
                    u = g * q["upg"] + uu
                    for st in range(USTEPS):
                        n = uu * USTEPS + st
                        cu, ct = (n - SPLIT_LAG) // USTEPS, (n - SPLIT_LAG) % USTEPS
                        split_here = live(q, cu, first, last) and not on_act(ct)
                        if split_here:
                            m = (g * q["upg"] + cu) * USTEPS + ct
                            v.wait_ge(s["p32"], m + 1)
                            if positive(q, g, cu, ct - RP, first):
                                v.wait_ge(s["av"], m - (RP - 1))
                            nc.vector.tensor_copy(PH[:, ct % RP, :], P32[:, ct % 4, :]).then_inc(s["phv"], 1)
                        mu, mpos = (n + MLEAD - 1) // USTEPS, (n + MLEAD - 1) % USTEPS
                        if live(q, mu, first, last):
                            mi = (g * q["upg"] + mu) * USTEPS + mpos
                            v.wait_ge(s["sm"], mi + 1)
                            nc.vector.reduce_max(MX[:, mu % 2, mpos:mpos + 1], PS[:, M_BANK + mpos % 2, :],
                                                 AX.X).then_inc(s["mx"], 1)
                        if split_here:
                            v.wait_ge(s["phv"], (g * q["upg"] + cu) * 4 + ct // 4 + 1)
                            nc.vector.tensor_tensor(PL[:, ct % RP, :], P32[:, ct % 4, :], PH[:, ct % RP, :],
                                                    ALU.subtract).then_inc(s["plv"], 1)
                        u1 = u + 1
                        if live(q, uu + 1, first, last) and st == q["m_nm"]:
                            v.wait_ge(s["mx"], u1 * USTEPS + USTEPS)
                            mx = MX[:, (uu + 1) % 2, :].rearrange("p (a b) -> p a b", b=4)
                            if not (first and uu + 1 < 1):
                                v.wait_ge(s["mt"], u1)
                            if q["kind"] == 0:
                                nc.vector.tensor_scalar(MT[:, :, 0:HPU].rearrange("p i j -> p j i"), mx,
                                                        -1.0 / MSC, None, ALU.mult).then_inc(s["nm"], 1)
                            else:
                                nc.vector.reduce_max(MR[:, :], mx, AX.X).then_inc(s["mr"], 1)
                                v.wait_ge(s["mr"], u1 + 1)
                                nc.vector.tensor_scalar(MT[:, :, 0], MR[:, :], -1.0 / MSC, None,
                                                        ALU.mult).then_inc(s["nm"], 1)
                        if live(q, uu + 1, first, last) and st == q["m_ev"]:
                            v.wait_ge(s["mt"], u1 + 1)
                            r = (uu + 1) % 4
                            if q["kind"] == 0:
                                nc.vector.tensor_copy(QA[96:P, r, :], PS[96:P, A_BANK, :]).then_inc(s["mrow"], 1)
                            else:
                                nc.vector.tensor_copy(QB[64:96, r, :], PS[64:96, A_BANK, :]).then_inc(s["mrow"], 1)
                        u2 = u + 2
                        if live(q, uu + 2, first, last):
                            r = (uu + 2) % 4
                            hg = (uu + 2) % q["upg"]
                            if q["kind"] == 0 and st == q["k_ev"]:
                                v.wait_ge(s["khi"], u2 + 1)
                                nc.vector.scalar_tensor_tensor(
                                    out=KR[64:96, :], in0=PS[64:96, A_BANK, :], scalar=BK0[64:96, hg:hg + 1],
                                    in1=KR[64:96, :], op0=ALU.add, op1=ALU.subtract).then_inc(s["klo"], 1)
                            if q["kind"] == 0 and st == q["k_ev"] + 1:
                                v.wait_ge(s["klo"], u2 + 1)
                                for j in range(HPU):
                                    nc.vector.tensor_scalar(KM[:, r, j, :], KR[:, :], MASK[:, j:j + 1], None,
                                                            ALU.mult).then_inc(s["km"], 1)
                            if q["kind"] == 0 and st == q["q_ev"]:
                                v.wait_ge(s["qhi"], u2 + 1)
                                nc.vector.scalar_tensor_tensor(
                                    out=QA[32:64, r, :], in0=PS[32:64, A_BANK, :], scalar=BQ0[32:64, hg:hg + 1],
                                    in1=QA[32:64, r, :], op0=ALU.add, op1=ALU.subtract).then_inc(s["qlo"], 1)
                            if q["kind"] == 0 and st == q["v_ev"]:
                                v.wait_ge(s["vp"], u2 + 1)
                                for i in range(TG):
                                    nc.vector.tensor_tensor(VF[:, i, :], PS[:, A_BANK, i * 32:(i + 1) * 32],
                                                            BV0[:, hg * 32:(hg + 1) * 32],
                                                            ALU.add).then_inc(s["vf"], 1)
                            if q["kind"] == 0 and st == q["v_ev"] + 1:
                                v.wait_ge(s["vf"], u2 * TG + TG)
                                vf = VF[:, :, :].rearrange("p t (j d) -> p t j d", d=D0)
                                nc.vector.tensor_copy(V0[:, r, :, :, D0:2 * D0], vf).then_inc(s["vhi"], 1)
                                v.wait_ge(s["vhi"], u2 + 1)
                                nc.vector.tensor_tensor(V0[:, r, :, :, 0:D0], vf, V0[:, r, :, :, D0:2 * D0],
                                                        ALU.subtract).then_inc(s["vlo"], 1)
                            if q["kind"] == 1 and st == q["q_ev"]:
                                v.wait_ge(s["qhi"], u2 + 1)
                                nc.vector.tensor_copy(QB[0:64, r, :], QA[0:64, r, :])
                                nc.vector.tensor_tensor(QA[64:P, r, :], PS[64:P, A_BANK, :], QA[64:P, r, :],
                                                        ALU.subtract).then_inc(s["qlo"], 1)
                        if live(q, uu - 1, first, last) and st in (q["o_post"], q["o_post"] + 1):
                            uo = u - 1
                            h = (uu - 1) % q["upg"]
                            dd = D0 if q["kind"] == 0 else D1
                            nh = HPU if q["kind"] == 0 else 1
                            os = OS[:, 0:TG * nh * (2 * dd + 1)].rearrange("p (t n) -> p t n", n=2 * dd + 1)
                            ot = OT[:, 0:TG * nh * dd].rearrange("p (t n) -> p t n", n=dd)
                            if st == q["o_post"]:
                                v.wait_ge(s["oev"], uo + 1)
                                nc.vector.reciprocal(RC[:, 0:TG * nh], os[:, :, 2 * dd]).then_inc(s["rc"], 1)
                                nc.vector.tensor_tensor(ot, os[:, :, 0:dd], os[:, :, dd:2 * dd],
                                                        ALU.add).then_inc(s["ot"], 1)
                            else:
                                v.wait_ge(s["rc"], uo + 1)
                                v.wait_ge(s["ot"], uo + 1)
                                if not first and uu >= 1 and (h == 0 if q["kind"] == 0 else h % 2 == 0):
                                    v.wait_ge(s["aot"], (g - 1) * q["rounds"] + (1 if q["kind"] == 0 else 1 + h // 2))
                                rc = RC[:, 0:TG * nh].rearrange("p (t o) -> p t o", o=1)\
                                    .broadcast_to([P, TG * nh, dd])
                                if q["kind"] == 0:
                                    for i in range(TG):
                                        ao = AO[:, i, h * 32:(h + 1) * 32].rearrange("p (j d) -> p j d", d=D0)
                                        last_i = nc.vector.tensor_tensor(
                                            ao, ot[:, i * nh:(i + 1) * nh, :], rc[:, i * nh:(i + 1) * nh, :], ALU.mult)
                                    last_i.then_inc(s["post"], 1)
                                else:
                                    nc.vector.tensor_tensor(AO[:, :, h * D1:(h + 1) * D1], ot, rc,
                                                            ALU.mult).then_inc(s["post"], 1)
                        pos = closing_pos(q, g, uu, first, last)
                        if pos:
                            gg, w = pos
                            xg = X[:, ds(gg * TG, TG), :]
                            pw = PS[:, W_BANK, :].rearrange("p (t c) -> p t c", c=C)

                            def wide(t):
                                return t[:, :].rearrange("p (o c) -> p o c", o=1).broadcast_to([P, TG, C])
                            if st == q["t_ev"] and w < q["rounds"]:
                                v.wait_ge(s["aohi"], gg * q["rounds"] + w + 1)
                                nc.vector.tensor_tensor(AOL[:, :], PS[:, A_BANK, :], AOH[:, :],
                                                        ALU.subtract).then_inc(s["aolo"], 1)
                            if w == q["x_w"] and st == q["x_s"]:
                                v.wait_ge(s["wo"], (gg + 1) * q["rounds"])
                                carry_v()
                                if q["kind"] == 0:
                                    nc.vector.tensor_tensor(xg, xg, pw, ALU.add).then_inc(s["x"], 1)
                                    v.wait_ge(s["x"], 2 * gg + 1)
                                    nc.vector.tensor_tensor(xg, xg, wide(BO0), ALU.add).then_inc(s["x"], 1)
                                else:
                                    for i in range(TG):
                                        nc.vector.bn_stats(BST[:, i, :], pw[:, i, :]).then_inc(s["ostat"], 1)
                                    v.wait_ge(s["ostat"], (gg + 1) * TG)
                                    carry_v()
                                    for i in range(TG):
                                        nc.vector.bn_aggr(MV[:, i, :], BST[:, i, :]).then_inc(s["oagg"], 1)
                            if q["kind"] == 1 and w == q["x_w"] and st == q["x_s"] + 2:
                                v.wait_ge(s["orstd"], gg + 1)
                                for i in range(TG):
                                    nc.vector.tensor_scalar(ON[:, i, :], pw[:, i, :], MV[:, i, 0:1], RS[:, i:i + 1],
                                                            ALU.subtract, ALU.mult).then_inc(s["on"], 1)
                            if q["kind"] == 1 and w == q["x_w"] and st == q["x_s"] + 3:
                                v.wait_ge(s["on"], gg * (TG + 2) + TG)
                                nc.vector.tensor_tensor(ON[:, :, :], ON[:, :, :], wide(ONW), ALU.mult)\
                                    .then_inc(s["on"], 1)
                            if q["kind"] == 1 and w == q["x_w"] and st == q["x_s"] + 4:
                                v.wait_ge(s["on"], gg * (TG + 2) + TG + 1)
                                nc.vector.tensor_tensor(ON[:, :, :], ON[:, :, :], wide(ONB), ALU.add)\
                                    .then_inc(s["on"], 1)
                            if q["kind"] == 1 and w == q["x_w"] and st == q["x_s"] + 5:
                                v.wait_ge(s["on"], gg * (TG + 2) + TG + 2)
                                nc.vector.tensor_tensor(xg, xg, ON[:, :, :], ALU.add).then_inc(s["x"], 1)
                            if w == q["st_w"] and st == q["st_s"]:
                                v.wait_ge(s["x"], 2 * gg + 2 if q["kind"] == 0 else gg + 1)
                                carry_v()
                                norm_stats(v, q["p"] + 1, gg)
                            if w == q["ap_w"] and st == q["ap_s"]:
                                norm_apply(v, q["p"] + 1, gg)
                            if w == q["tr_w"] and st == q["lo_s"]:
                                norm_lo(v, q["p"] + 1, gg, W_BANK)

            def prelude1(base):
                for i4 in range(q["groups"]):
                    gg = base + i4
                    v.wait_ge(s["khi"], gg + 1)
                    nc.vector.tensor_tensor(KB[0:64, ds(i4 * GT, GT)], PS[0:64, A_BANK, :],
                                            KA[0:64, ds(i4 * GT, GT)], ALU.subtract).then_inc(s["kfree"], 1)
                    v.wait_ge(s["vhi"], gg + 1)
                    nc.vector.tensor_tensor(V1[:, ds(i4 * TG, TG), 0:D1],
                                            PS[:, W_BANK, 0:TG * D1].rearrange("p (t d) -> p t d", d=D1),
                                            V1[:, ds(i4 * TG, TG), D1:2 * D1],
                                            ALU.subtract).then_inc(s["vfree"], 1)
            att_run(v, q, body, prelude1 if q["kind"] == 1 else None)

        ffn_s = sems("ffn", "gu sg prod hi h down yt ft x")
        moe_s = sems("moe", "gu g u uc sg a b prod hi h down yt ft x lg lgs t8 dl i8 ifl th w12 sa sc "
                            "s16h s16 st s2")
        shared = "sm mx nm mt mrow st p32 pha phv plp plv av oev rc ot post aot aohi aolo wo x qp qhi qlo kp khi vp vhi "
        att_s = [sems("att0", shared + "klo km vf vlo"),
                 sems("att1", shared + "kfree vfree mr ostat oagg ovar orstd on")]
        q0, q1 = att(0), att(1)

        pieces = [
            *[(WQ0[0][:, :, r, :], WQ0[1][:, :, r, :], RQKV[:, 0, :, :]) for r in range(3)],
            *[(WK0[0][:, :, r, :], WK0[1][:, :, r, :], RQKV[:, 1, :, :]) for r in range(3)],
            (WV0[0][:, :], WV0[1][:, :], RQKV[:, 2, :, :].rearrange("p h d -> p (h d)")),
            (WO0[0][:, :], WO0[1][:, :], RWO0[:, :]),
            (MG[0][:, :, :, :].rearrange("p a b i -> p (a b) i"), MG[1][:, :, :, :].rearrange("p a b i -> p (a b) i"),
             RGU[:, :, 0:2 * I1:2]),
            (MU[0][:, :, :, :].rearrange("p a b i -> p (a b) i"), MU[1][:, :, :, :].rearrange("p a b i -> p (a b) i"),
             RGU[:, :, 1:2 * I1:2]),
            (MD[0][:, :, :], MD[1][:, :, :], RMD[:, :, :]),
            (RT[0][:, :], RT[1][:, :], RRT[:, :]),
            *[(WQ1[0][:, :, r, :], WQ1[1][:, :, r, :], RWQ1[:, :, :]) for r in range(2)],
            *[(WK1[0][:, r, :], WK1[1][:, r, :], RKV1[:, 0, :]) for r in range(2)],
            (WV1[0][:, :], WV1[1][:, :], RKV1[:, 1, :]),
            (WO1[0][:, :, :], WO1[1][:, :, :], RWO1[:, :, :]),
            (BD[0][:, :], BD[1][:, :], BDR[:, :]),
        ]

        ctx.enter_context(nc.allow_non_contiguous_dma(reason="a few hundred bias values, one to a partition"))
        block = ctx.enter_context(nc.Block())

        @block.sync
        def _(sp):
            for g in range(2):
                sp.dma_start(X[:, g * TG:(g + 1) * TG, :], x_dram(d["L0_attn_x"], g)).then_inc(ld_x[g], 16)

            def expert(e):
                w = WST[:, e % 4, :, :]
                sp.dma_start(w[:, 0, :], d["L0_ffn_Wg"][e]).then_inc(ld_e[e], 16)
                sp.dma_start(w[:, 1, :], d["L0_ffn_Wu"][e]).then_inc(ld_e[e], 16)
                sp.dma_start(w[:, 2, :].rearrange("p (f c) -> p f c", c=C),
                             d["L0_ffn_Wd"][e].rearrange("(f p) c -> p f c", p=P)).then_inc(ld_e[e], 16)
            for e in range(4):
                expert(e)
            for g in range(2, NG):
                sp.dma_start(X[:, g * TG:(g + 1) * TG, :], x_dram(d["L0_attn_x"], g)).then_inc(ld_x[g], 16)
            for e in range(4, E0):
                sp.wait_ge(c["elo"], e - 3)
                expert(e)
            w = d["L0_attn_w_qkv"].rearrange("c (a h n) -> c a h n", a=3, n=32)
            sp.dma_start(RQKV[:, :, :, :], w).then_inc(ld_w, 16)
            sp.dma_start(RWO0[:, :], d["L0_attn_w_o"]).then_inc(ld_w, 16)
            sp.dma_start(RGU[:, :, :], d["L1_ffn_gate_up_proj"].rearrange("e h f -> h e f")).then_inc(ld_w, 16)
            sp.dma_start(RMD[:, :, :], d["L1_ffn_down_proj"].rearrange("(j e) i h -> (e i) j h", e=2))\
                .then_inc(ld_w, 16)
            sp.dma_start(RRT[:, :], d["L1_ffn_router_weight"]).then_inc(ld_w, 16)
            sp.dma_start(RWQ1[:, :, :], d["L1_attn_Wq"].rearrange("c (h n) -> c h n", n=D1)).then_inc(ld_w, 16)
            sp.dma_start(RKV1[:, :, :], d["L1_attn_Wkv"].rearrange("c (a n) -> c a n", n=D1)).then_inc(ld_w, 16)
            sp.dma_start(RWO1[:, :, :], d["L1_attn_Wo"].rearrange("(r p) c -> p r c", p=P)).then_inc(ld_w, 16)
            for g in range(NG):
                sp.wait_ge(moe_s["x"], NG + g + 1)
                sp.dma_start(x_dram(d["out"], g), X[:, g * TG:(g + 1) * TG, :]).then_inc(out_done, 16)
            sp.wait_ge(out_done, 16 * NG)

        @block.gpsimd
        def _(pool):
            g_ = nc.gpsimd
            g_.memset(ID32[:, :], 0.0).then_inc(c["zero"], 1)
            g_.memset(ID16[:, :], 0.0).then_inc(c["zero"], 1)
            g_.memset(NHALF[:, :], -0.5).then_inc(c["zero"], 1)
            pool.wait_ge(c["zero"], 3)
            for t in (ID32, ID16):
                g_.affine_select(out=t[:, :], in_=t[:, :], compare_op=ALU.not_equal, fill=1.0, base=0,
                                 pattern=[[-1, P]], channel_multiplier=1).then_inc(c["idn"], 1)
            for g in range(NG):
                norm_rstd(pool, 0, g)
            for e in range(E0):
                pool.wait_ge(c["ehi"], 3 * e + 3)
                for a, (w, sh) in enumerate(((WG, None), (WU, None), (WD, 1))):
                    hi, lo = (t[:, e, :] if sh is None else t[:, e, :, :].rearrange("p f c -> p (f c)") for t in w)
                    last = g_.tensor_tensor(lo, WST[:, e % 4, a, :], hi, ALU.subtract)
                last.then_inc(c["elo"], 1)
            pool.wait_ge(c["pad"], 11)
            sel = SEL[:, :, :, :].rearrange("p a b i -> p (a b) i")
            for b in (0, 64):
                g_.affine_select(out=sel, in_=sel, compare_op=ALU.not_equal, fill=1.0, base=-b,
                                 pattern=[[-1, E1], [0, I1]], channel_multiplier=1).then_inc(c["pool"], 1)
                pool.wait_ge(c["pool"], 1 if b == 0 else 2)
            m3 = MASK4[:, 0:3, :]
            g_.affine_select(out=m3, in_=m3, compare_op=ALU.is_ge, fill=0.0, base=0,
                             pattern=[[-32, 3], [-D0, HPU]], channel_multiplier=1).then_inc(c["pool"], 1)
            pool.wait_ge(c["pool"], 3)
            g_.affine_select(out=m3, in_=m3, compare_op=ALU.is_ge, fill=0.0, base=D0 - 1,
                             pattern=[[32, 3], [D0, HPU]], channel_multiplier=-1).then_inc(c["pool"], 1)
            g_.affine_select(out=MASK4[:, 3, :], in_=MASK4[:, 3, :], compare_op=ALU.is_equal, fill=0.0, base=-96,
                             pattern=[[-1, HPU]], channel_multiplier=1).then_inc(c["pool"], 1)
            for e in range(E1):
                g_.memset(IOTA[:, e:e + 1], float(e)).then_inc(c["iota"], 1)
            norms_pool(pool, 1)
            for i, (hi, lo, raw) in enumerate(pieces):
                pool.wait_ge(c["whi"], i + 1)
                g_.tensor_tensor(lo, raw, hi, ALU.subtract).then_inc(c["wlo"], 1)
            pool.wait_ge(c["wlo"], len(pieces))
            att_pool(pool, att_s[0], q0)
            drained(pool, 2)
            norms_pool(pool, 3)
            drained(pool, 3)
            moe_pool(pool, moe_s, 3, 0)
            att_pool(pool, att_s[1], q1)
            drained(pool, 5)
            moe_pool(pool, moe_s, 5, NG)

        @block.scalar
        def _(act):
            bq = d["L0_attn_b_qkv"].rearrange("(a h n) -> a n h", a=3, n=32)
            for r in range(3):
                act.dma_start(BQ0[32 * r:32 * r + 32, :], bq[0]).then_inc(ld_c, 16)
                act.dma_start(BK0[32 * r:32 * r + 32, :], bq[1]).then_inc(ld_c, 16)
            act.dma_start(BV0[:, :], d["L0_attn_b_qkv"][2 * C:3 * C].partition_broadcast(P)).then_inc(ld_c, 16)
            act.dma_start(BO0[:, :], d["L0_attn_b_o"].partition_broadcast(P)).then_inc(ld_c, 16)
            act.dma_start(ONW[:, :], d["L1_attn_out_norm_w"].partition_broadcast(P)).then_inc(ld_c, 16)
            act.dma_start(ONB[:, :], d["L1_attn_out_norm_b"].partition_broadcast(P)).then_inc(ld_c, 16)
            act.dma_start(NW[:, :], d["L1_attn_norm_w"].rearrange("(c o) -> c o", o=1)).then_inc(ld_c, 16)
            act.dma_start(NB[:, :], d["L1_attn_norm_b"].rearrange("(c o) -> c o", o=1)).then_inc(ld_c, 16)
            gb = d["L1_ffn_gate_up_proj_bias"].rearrange("(j e) (i two) -> two e i j", e=2, two=2)
            for e in range(2):
                act.dma_start(BG[64 * e:64 * e + 64, :], gb[0][e]).then_inc(ld_c, 16)
                act.dma_start(BU[64 * e:64 * e + 64, :], gb[1][e]).then_inc(ld_c, 16)
            for g in range(NG):
                norm_hi(act, 0, g, N_BANK)
            for e in range(E0):
                act.wait_ge(ld_e[e], 48)
                for a, w in enumerate((WG, WU, WD)):
                    hi = w[0][:, e, :] if a < 2 else w[0][:, e, :, :].rearrange("p f c -> p (f c)")
                    nc.scalar.copy(hi, WST[:, e % 4, a, :]).then_inc(c["ehi"], 1)
            act.wait_ge(c["pad"], 11)
            act.dma_start(BDR[0:E1, :], d["L1_ffn_down_proj_bias"]).then_inc(ld_c, 16)
            act.dma_start(BDR[64:64 + E1, :], d["L1_ffn_down_proj_bias"]).then_inc(ld_c, 16)
            ffn_act(act, ffn_s, 0, 0)
            att_act(act, att_s[0], q0)
            drained(act, 2)
            ffn_act(act, ffn_s, 2, NG)
            drained(act, 3)
            moe_act(act, moe_s, 3, 0)
            att_act(act, att_s[1], q1)
            drained(act, 5)
            moe_act(act, moe_s, 5, NG)

        @block.vector
        def _(v):
            nc.vector.memset(SPARE[0][:, :], 0.0).then_inc(c["pad"], 1)
            for k in (WQ0[0], WQ0[1], WK0[0], WK0[1]):
                nc.vector.memset(k[:, :, 3, :], 0.0).then_inc(c["pad"], 1)
            nc.vector.memset(BQ0[96:P, :], 0.0).then_inc(c["pad"], 1)
            nc.vector.memset(BK0[96:P, :], MSC).then_inc(c["pad"], 1)
            nc.vector.memset(SEL[:, :, :, :], 0.0).then_inc(c["pad"], 1)
            nc.vector.memset(MASK4[:, :, :], 1.0).then_inc(c["pad"], 1)
            nc.vector.memset(BDR[:, :], 0.0).then_inc(c["pad"], 1)
            nc.vector.memset(BD[1][:, :], 0.0).then_inc(c["pad"], 1)
            v.wait_ge(c["pad"], 1)
            for g in range(NG):
                v.wait_ge(ld_x[g], 16)
                norm_stats(v, 0, g)
                norm_apply(v, 0, g)
                norm_lo(v, 0, g, N_BANK)
            ffn_dve(v, ffn_s, 0, 0)
            v.wait_ge(ld_w, 16 * N_LDW)
            v.wait_ge(ld_c, 16 * (N_LDC + 1))
            v.wait_ge(c["pool"], 5)
            nc.vector.tensor_scalar(BU1[:, :], BU[:, :], 1.0, None, ALU.add).then_inc(c["bias"], 1)
            nc.vector.reduce_sum(MASK[:, :], MASK4[:, :, :].rearrange("p r j -> p j r"), AX.X).then_inc(c["mask"], 1)
            for hi, lo, raw in pieces:
                nc.vector.tensor_copy(hi, raw).then_inc(c["whi"], 1)
            v.wait_ge(c["wlo"], len(pieces))
            v.wait_ge(c["mask"], 1)
            v.wait_ge(c["bias"], 1)
            nc.vector.memset(V0[:, :, :, :, 2 * D0:2 * D0 + 1], 1.0)
            nc.vector.memset(MT[:, :, :], 0.0).then_inc(c["one"], 1)
            v.wait_ge(c["one"], 1)
            att_dve(v, att_s[0], q0)
            ffn_dve(v, ffn_s, 2, NG)
            nc.vector.memset(S16[:, :, :], 0.0).then_inc(c["one"], 1)
            v.wait_ge(c["one"], 2)
            moe_dve(v, moe_s, 3, 0)
            nc.vector.memset(V1[:, :, 2 * D1:2 * D1 + 1], 1.0)
            nc.vector.memset(KB[64:96, :], 0.0).then_inc(c["one"], 1)
            nc.vector.memset(MT[:, :, :], 0.0).then_inc(c["one"], 1)
            v.wait_ge(c["one"], 4)
            nc.vector.memset(KB[64:65, :], MSC).then_inc(c["one"], 1)
            v.wait_ge(c["one"], 5)
            att_dve(v, att_s[1], q1)
            nc.vector.memset(S16[:, :, :], 0.0).then_inc(c["one"], 1)
            v.wait_ge(c["one"], 6)
            moe_dve(v, moe_s, 5, NG)

        @block.tensor
        def _(pe):
            pe.wait_ge(c["idn"], 2)
            for g in range(NG):
                norm_transpose(pe, 0, g, N_BANK)
            ffn_pe(pe, ffn_s, 0, 0)
            pe.wait_ge(c["wlo"], len(pieces))
            pe.wait_ge(c["one"], 1)
            att_pe(pe, att_s[0], q0)
            drained(pe, 2)
            ffn_pe(pe, ffn_s, 2, NG)
            drained(pe, 3)
            moe_pe(pe, moe_s, 3, 0)
            pe.wait_ge(c["one"], 5)
            att_pe(pe, att_s[1], q1)
            drained(pe, 5)
            moe_pe(pe, moe_s, 5, NG)


_OUT = (BATCH, SEQ, C)


def kernel(**inputs):
    import numpy as np
    import concourse.bacc as bacc
    from concourse.bass_utils import run_bass_kernel_spmd

    nc = bacc.Bacc("TRN2", target_bir_lowering=False, num_devices=1)
    arrays, aps = {}, {}
    for name, a in inputs.items():
        a = np.ascontiguousarray(a)
        arrays[f"in_{name}"] = a
        aps[name] = nc.dram_tensor(f"in_{name}", a.shape, mybir.dt.from_np(a.dtype), kind="ExternalInput").ap()
    aps["out"] = nc.dram_tensor("out_0", _OUT, F32, kind="ExternalOutput").ap()
    program(nc, aps)
    r = run_bass_kernel_spmd(nc, [arrays], core_ids=[0])
    return r.results[0]["out_0"]
```
